# Optimizing a Trainium2 kernel written in Bass

```python
import numpy as np
import jax
import jax.numpy as jnp

def _softmax(x, axis=-1):
    return jax.nn.softmax(x, axis=axis)

def _gelu(x):
    return jax.nn.gelu(x, approximate=True)

def _silu(x):
    return jax.nn.silu(x)

def _sigmoid(x):
    return jax.nn.sigmoid(x)

def _layernorm(x, axis=-1, eps=1e-05):
    m = jnp.mean(x, axis=axis, keepdims=True)
    v = jnp.var(x, axis=axis, keepdims=True)
    return (x - m) / jnp.sqrt(v + eps)

def _scatter_add(tgt, idx, src, axis=0):
    return tgt.at[idx].add(src)

def _segment_sum(src, seg, n):
    return jax.ops.segment_sum(src, seg, n)
kernel_name = 'mk_recurrent_d1_jaxref_r4_3e0519'

def setup_inputs(seed: int=0):
    np.random.seed(seed)
    _w = jnp.asarray

    def _L0_attn_setup():
        import jax, jax.numpy as jnp
        import numpy as np
        EMBED_DIM = 512
        NUM_HEADS = 16
        HEAD_DIM = EMBED_DIM // NUM_HEADS
        BASE = 10000.0

        def rotate_half(x):
            half = x.shape[-1] // 2
            x1, x2 = (x[..., :half], x[..., half:])
            return jnp.concatenate([-x2, x1], axis=-1)

        def apply_rope(x, base=BASE):
            S, Dh = (x.shape[-2], x.shape[-1])
            inv_freq = 1.0 / base ** (jnp.arange(0, Dh, 2, dtype=jnp.float32) / Dh)
            t = jnp.arange(S, dtype=jnp.float32)
            freqs = jnp.einsum('i,j->ij', t, inv_freq)
            emb = jnp.concatenate([freqs, freqs], axis=-1)
            return x * jnp.cos(emb) + rotate_half(x) * jnp.sin(emb)
        key = jax.random.key(seed)
        ks = jax.random.split(key, 9)
        B, S, D = (2, 512, EMBED_DIM)
        xavier = lambda k, shape: jax.random.uniform(k, shape, jnp.float32, -1.0, 1.0) * float(np.sqrt(6.0 / (shape[0] + shape[1])))
        return {'x': jax.random.normal(ks[0], (B, S, D), jnp.float32), 'q_w': xavier(ks[1], (D, D)), 'k_w': xavier(ks[2], (D, D)), 'v_w': xavier(ks[3], (D, D)), 'q_b': jnp.zeros((D,), jnp.float32), 'k_b': jnp.zeros((D,), jnp.float32), 'v_b': jnp.zeros((D,), jnp.float32), 'out_w': xavier(ks[4], (D, D)), 'out_b': jnp.zeros((D,), jnp.float32)}
    _L0_attn_in = _L0_attn_setup()

    def _L0_ffn_setup():
        import jax, jax.numpy as jnp
        import numpy as np
        B, S, H = (2, 512, 512)
        E, G, TKG, K = (32, 8, 4, 8)
        I, SI = (256, 512)
        ROUTED_SCALE = 2.5

        def _moe_forward(hidden_states, router_w, router_bias, w_gate, w_up, w_down, sw_gate, sw_up, sw_down):
            x = hidden_states.reshape(-1, H)
            T = x.shape[0]
            logits = x.astype(jnp.float32) @ router_w.astype(jnp.float32)
            scores = jax.nn.sigmoid(logits)
            scores_grouped = (scores + router_bias).reshape(T, G, E // G)
            top2, _ = jax.lax.top_k(scores_grouped, 2)
            group_scores = top2.sum(-1)
            _, top_groups = jax.lax.top_k(group_scores, TKG)
            mask = jnp.ones((T, G), bool).at[jnp.arange(T)[:, None], top_groups].set(False)
            masked = jnp.where(mask[:, :, None], 0.0, scores_grouped).reshape(T, E)
            _, top_k_index = jax.lax.top_k(masked, K)
            tkw = jnp.take_along_axis(scores, top_k_index, axis=-1)
            tkw = tkw / tkw.sum(-1, keepdims=True)
            tkw = (tkw * ROUTED_SCALE).astype(hidden_states.dtype)
            flat_idx = top_k_index.reshape(-1)
            sort_idx = jnp.argsort(flat_idx)
            xs = jnp.repeat(x, K, axis=0)[sort_idx]
            group_sizes = jnp.bincount(flat_idx, length=E).astype(jnp.int32)
            gate = jax.lax.ragged_dot(xs, w_gate, group_sizes)
            up = jax.lax.ragged_dot(xs, w_up, group_sizes)
            down = jax.lax.ragged_dot(jax.nn.silu(gate) * up, w_down, group_sizes)
            unsort = jnp.argsort(sort_idx)
            routed = (down[unsort].reshape(T, K, H) * tkw[..., None]).sum(axis=1)
            shared = jax.nn.silu(x @ sw_gate) * (x @ sw_up) @ sw_down
            return (routed + shared).reshape(hidden_states.shape)
        key = jax.random.key(seed)
        ks = jax.random.split(key, 9)

        def w(k, shape, fan_in):
            return jax.random.normal(k, shape, jnp.float32) / np.float32(np.sqrt(fan_in))
        return dict(hidden_states=jax.random.normal(ks[0], (B, S, H), jnp.float32), router_w=w(ks[1], (H, E), H), router_bias=jnp.zeros((E,), jnp.float32), w_gate=w(ks[2], (E, H, I), H), w_up=w(ks[3], (E, H, I), H), w_down=w(ks[4], (E, I, H), I), sw_gate=w(ks[5], (H, SI), H), sw_up=w(ks[6], (H, SI), H), sw_down=w(ks[7], (SI, H), SI))
    _L0_ffn_in = _L0_ffn_setup()
    _d = {'L0_attn_x': _L0_attn_in['x'], 'L0_attn_q_w': _L0_attn_in['q_w'], 'L0_attn_k_w': _L0_attn_in['k_w'], 'L0_attn_v_w': _L0_attn_in['v_w'], 'L0_attn_q_b': _L0_attn_in['q_b'], 'L0_attn_k_b': _L0_attn_in['k_b'], 'L0_attn_v_b': _L0_attn_in['v_b'], 'L0_attn_out_w': _L0_attn_in['out_w'], 'L0_attn_out_b': _L0_attn_in['out_b'], 'L0_ffn_router_w': _L0_ffn_in['router_w'], 'L0_ffn_router_bias': _L0_ffn_in['router_bias'], 'L0_ffn_w_gate': _L0_ffn_in['w_gate'], 'L0_ffn_w_up': _L0_ffn_in['w_up'], 'L0_ffn_w_down': _L0_ffn_in['w_down'], 'L0_ffn_sw_gate': _L0_ffn_in['sw_gate'], 'L0_ffn_sw_up': _L0_ffn_in['sw_up'], 'L0_ffn_sw_down': _L0_ffn_in['sw_down']}
    _x0 = _d['L0_attn_x']
    _d['L0_attn_x'] = jax.random.normal(jax.random.fold_in(jax.random.key(seed), 1), (4, 512, 512), dtype=_x0.dtype)
    del _x0
    return _d

def reference(L0_attn_x, L0_attn_q_w, L0_attn_k_w, L0_attn_v_w, L0_attn_q_b, L0_attn_k_b, L0_attn_v_b, L0_attn_out_w, L0_attn_out_b, L0_ffn_router_w, L0_ffn_router_bias, L0_ffn_w_gate, L0_ffn_w_up, L0_ffn_w_down, L0_ffn_sw_gate, L0_ffn_sw_up, L0_ffn_sw_down):

    def _L0_attn_ref(x, q_w, k_w, v_w, q_b, k_b, v_b, out_w, out_b):
        import jax, jax.numpy as jnp
        import numpy as np
        EMBED_DIM = 512
        NUM_HEADS = 16
        HEAD_DIM = EMBED_DIM // NUM_HEADS
        BASE = 10000.0

        def rotate_half(x):
            half = x.shape[-1] // 2
            x1, x2 = (x[..., :half], x[..., half:])
            return jnp.concatenate([-x2, x1], axis=-1)

        def apply_rope(x, base=BASE):
            S, Dh = (x.shape[-2], x.shape[-1])
            inv_freq = 1.0 / base ** (jnp.arange(0, Dh, 2, dtype=jnp.float32) / Dh)
            t = jnp.arange(S, dtype=jnp.float32)
            freqs = jnp.einsum('i,j->ij', t, inv_freq)
            emb = jnp.concatenate([freqs, freqs], axis=-1)
            return x * jnp.cos(emb) + rotate_half(x) * jnp.sin(emb)
        B, S, D = x.shape
        H, Dh = (NUM_HEADS, HEAD_DIM)
        scaling = Dh ** (-0.5)
        q = (x @ q_w.T + q_b).reshape(B, S, H, Dh).transpose(0, 2, 1, 3)
        k = (x @ k_w.T + k_b).reshape(B, S, H, Dh).transpose(0, 2, 1, 3)
        v = (x @ v_w.T + v_b).reshape(B, S, H, Dh).transpose(0, 2, 1, 3)
        q = apply_rope(q)
        k = apply_rope(k)
        attn = jnp.einsum('bhqd,bhkd->bhqk', q, k) * scaling
        probs = jax.nn.softmax(attn, axis=-1)
        out = jnp.einsum('bhqk,bhkd->bhqd', probs, v)
        out = out.transpose(0, 2, 1, 3).reshape(B, S, D)
        return out @ out_w.T + out_b

    def _L0_ffn_ref(hidden_states, router_w, router_bias, w_gate, w_up, w_down, sw_gate, sw_up, sw_down):
        import jax, jax.numpy as jnp
        import numpy as np
        B, S, H = (2, 512, 512)
        E, G, TKG, K = (32, 8, 4, 8)
        I, SI = (256, 512)
        ROUTED_SCALE = 2.5

        def _moe_forward(hidden_states, router_w, router_bias, w_gate, w_up, w_down, sw_gate, sw_up, sw_down):
            x = hidden_states.reshape(-1, H)
            T = x.shape[0]
            logits = x.astype(jnp.float32) @ router_w.astype(jnp.float32)
            scores = jax.nn.sigmoid(logits)
            scores_grouped = (scores + router_bias).reshape(T, G, E // G)
            top2, _ = jax.lax.top_k(scores_grouped, 2)
            group_scores = top2.sum(-1)
            _, top_groups = jax.lax.top_k(group_scores, TKG)
            mask = jnp.ones((T, G), bool).at[jnp.arange(T)[:, None], top_groups].set(False)
            masked = jnp.where(mask[:, :, None], 0.0, scores_grouped).reshape(T, E)
            _, top_k_index = jax.lax.top_k(masked, K)
            tkw = jnp.take_along_axis(scores, top_k_index, axis=-1)
            tkw = tkw / tkw.sum(-1, keepdims=True)
            tkw = (tkw * ROUTED_SCALE).astype(hidden_states.dtype)
            flat_idx = top_k_index.reshape(-1)
            sort_idx = jnp.argsort(flat_idx)
            xs = jnp.repeat(x, K, axis=0)[sort_idx]
            group_sizes = jnp.bincount(flat_idx, length=E).astype(jnp.int32)
            gate = jax.lax.ragged_dot(xs, w_gate, group_sizes)
            up = jax.lax.ragged_dot(xs, w_up, group_sizes)
            down = jax.lax.ragged_dot(jax.nn.silu(gate) * up, w_down, group_sizes)
            unsort = jnp.argsort(sort_idx)
            routed = (down[unsort].reshape(T, K, H) * tkw[..., None]).sum(axis=1)
            shared = jax.nn.silu(x @ sw_gate) * (x @ sw_up) @ sw_down
            return (routed + shared).reshape(hidden_states.shape)
        return _moe_forward(hidden_states, router_w, router_bias, w_gate, w_up, w_down, sw_gate, sw_up, sw_down)
    x = L0_attn_x
    xn = _layernorm(x, axis=-1)
    s = _L0_attn_ref(xn, L0_attn_q_w, L0_attn_k_w, L0_attn_v_w, L0_attn_q_b, L0_attn_k_b, L0_attn_v_b, L0_attn_out_w, L0_attn_out_b)
    g = _silu(_L0_ffn_ref(xn, L0_ffn_router_w, L0_ffn_router_bias, L0_ffn_w_gate, L0_ffn_w_up, L0_ffn_w_down, L0_ffn_sw_gate, L0_ffn_sw_up, L0_ffn_sw_down))
    x = x + s * g
    return x

_drawn_inputs = setup_inputs


def setup_inputs(seed=0):
    import zlib

    import numpy as np

    out = dict(_drawn_inputs(seed))
    spreads = {'L0_attn_q_b': (0.0, 0.8),
     'L0_attn_k_b': (0.0, 0.8),
     'L0_attn_v_b': (0.0, 0.1),
     'L0_attn_out_b': (0.0, 0.1),
     'L0_ffn_router_bias': (0.0, 0.1)}
    factors = {}
    for name, (base, spread) in spreads.items():
        noise = np.random.default_rng([zlib.crc32(name.encode()), seed]).standard_normal(out[name].shape)
        drawn = base * np.exp(spread * noise) if base else spread * noise
        out[name] = jnp.asarray(drawn.astype(out[name].dtype))
    for name, factor in factors.items():
        out[name] = (out[name] * factor).astype(out[name].dtype)
    return out
```

```python
from contextlib import ExitStack

import concourse.bass as bass
import numpy as np
from concourse import mybir

F32 = mybir.dt.float32
F32R = mybir.dt.float32r
I32 = mybir.dt.int32
U32 = mybir.dt.uint32
ALU = mybir.AluOpType
ACT = mybir.ActivationFunctionType
AX = mybir.AxisListType

P = 128
BATCH, SEQ, D = 4, 512, 512
TOKENS = BATCH * SEQ
TB = SEQ // P
NBLK = TOKENS // P
KC = D // P
HEADS, DH = 16, 32
HALF = DH // 2
SCALE = float(DH) ** -0.5
E, GROUPS, GSEL, TOPK = 32, 8, 4, 8
EPG = E // GROUPS
INNER = 256
ROUTED_SCALE = 2.5
EPS = 1e-5
TILES = TOKENS * TOPK // P + E
SLOTS = TILES * P
WCOLS = KC * 2 * INNER + 2 * D
WRING = 4
STACK = 3 * DH
VW = 2 * DH
NONE = -3.0e38


def layer_kernel(nc, x, wqk, wv, wo, bqk, bv, bo, rw, rbias, wexp, swg, swu, swd,
                 cos, sin, ident, before_tok, before_e, before_g, iota_p, iota_t, iota_e, out):
    x_b = x.rearrange("b (t p) d -> b p t d", p=P)
    out_b = out.rearrange("b (t p) d -> (b t) p d", p=P)
    x_blk = x.rearrange("b (t p) d -> (b t) p d", p=P)

    q_stack = nc.dram_tensor("q_stack", (BATCH * HEADS, STACK, SEQ), F32).ap()
    k_stack = nc.dram_tensor("k_stack", (BATCH * HEADS, STACK, SEQ), F32).ap()
    v_dram = nc.dram_tensor("v_dram", (BATCH * HEADS, P, TB, VW), F32).ap()
    shared_dram = nc.dram_tensor("shared_dram", (NBLK, P, D), F32).ap()
    attn_dram = nc.dram_tensor("attn_dram", (NBLK, P, D), F32).ap()
    xs_dram = nc.dram_tensor("xs_dram", (SLOTS, D), F32).ap()
    ys_dram = nc.dram_tensor("ys_dram", (SLOTS, D), F32).ap()

    top = ExitStack()
    with top:
        def sem(name):
            return top.enter_context(nc.semaphore(name))

        def sbuf(stack, name, shape, dt=F32):
            return stack.enter_context(nc.sbuf_tensor(name, shape, dt))

        def psum(stack, name, shape, dt=F32):
            return stack.enter_context(nc.psum_tensor(name, shape, dt))

        slot8 = sbuf(top, "slot8", [P, NBLK, TOPK], U32)
        weight8 = sbuf(top, "weight8", [P, NBLK, TOPK])
        tile_slot = sbuf(top, "tile_slot", [1, TILES], I32)
        tile_need = sbuf(top, "tile_need", [1, TILES], I32)
        ring_need = sbuf(top, "ring_need", [1, E], I32)
        id_f = sbuf(top, "id_f", [P, P])
        id_r = sbuf(top, "id_r", [P, P], F32R)
        spread = sem("spread")

        mid = ExitStack()
        with mid:
            xn = sbuf(mid, "xn", [P, NBLK, D])
            logits = sbuf(mid, "logits", [P, NBLK, E])
            pad_slot = sbuf(mid, "pad_slot", [P, E], U32)

            with ExitStack() as st:
                project_stage(nc, st, sbuf, psum, x_b, xn, logits, wqk, wv, bqk, bv, rw, swg, swu, swd,
                              cos, sin, ident, id_f, id_r, q_stack, k_stack, v_dram, shared_dram)
            with ExitStack() as st:
                route_stage(nc, st, sbuf, psum, logits, rbias, before_tok, before_e, before_g,
                            iota_p, iota_t, iota_e, slot8, weight8, pad_slot, tile_slot, tile_need, ring_need)
            with ExitStack() as st:
                attend_stage(nc, st, sbuf, psum, q_stack, k_stack, v_dram, wo, bo, attn_dram, id_r,
                             xn, slot8, pad_slot, xs_dram, spread)
        with ExitStack() as st:
            experts_stage(nc, st, sbuf, psum, xs_dram, ys_dram, wexp, id_f, id_r,
                          tile_slot, tile_need, ring_need)
        with ExitStack() as st:
            combine_stage(nc, st, sbuf, slot8, weight8, ys_dram, shared_dram, attn_dram, x_blk, out_b)


def project_stage(nc, st, sbuf, psum, x_b, xn, logits, wqk, wv, bqk, bv, rw, swg, swu, swd,
                  cos, sin, ident, id_f, id_r, q_stack, k_stack, v_dram, shared_dram):
    def sem(name):
        return st.enter_context(nc.semaphore(name))

    mats = [wqk[0], wqk[1], wv, swg, swu, swd]
    WQ, WK, WV, WG, WU, WD = range(6)
    NM = len(mats)
    w_hi = [sbuf(st, f"w_hi{m}", [P, KC, D], F32R) for m in range(NM)]
    w_lo = [sbuf(st, f"w_lo{m}", [P, KC, D], F32R) for m in range(NM)]
    w_raw = [sbuf(st, f"w_raw{i}", [P, KC, D]) for i in range(2)]
    rw_sb = sbuf(st, "rw_sb", [P, KC, E])
    cos_sb = sbuf(st, "cos_sb", [P, SEQ])
    sin_sb = sbuf(st, "sin_sb", [P, SEQ])
    bqk_sb = sbuf(st, "bqk_sb", [P, 2, KC])
    bv_sb = sbuf(st, "bv_sb", [P, D])
    xt_hi = sbuf(st, "xt_hi", [P, KC, SEQ], F32R)
    xt_lo = sbuf(st, "xt_lo", [P, KC, SEQ], F32R)
    ht_hi = sbuf(st, "ht_hi", [P, KC, SEQ], F32R)
    ht_lo = sbuf(st, "ht_lo", [P, KC, SEQ], F32R)
    stats = sbuf(st, "stats", [P, TB, 6])
    mv = sbuf(st, "mv", [P, TB, 2])
    var = sbuf(st, "var", [P, TB])
    rs = sbuf(st, "rs", [P, TB])
    rt = sbuf(st, "rt", [P, TB])
    power = sbuf(st, "power", [P, TB])
    half_sb = [sbuf(st, f"half_sb{i}", [P, SEQ]) for i in range(2)]
    rope_t = [sbuf(st, f"rope_t{i}", [P, SEQ]) for i in range(3)]
    rot = [rope_t[0], rope_t[2]]
    rot_hi = [sbuf(st, f"rot_hi{i}", [P, SEQ], F32R) for i in range(2)]
    rot_lo = [sbuf(st, f"rot_lo{i}", [P, SEQ], F32R) for i in range(2)]
    v_sb = [w_raw[0][:, 2 * i:2 * i + 2, :].rearrange("p a c -> p (a c)").rearrange("p (h d) -> p h d", h=HEADS)
            for i in range(2)]
    y_sb = [w_raw[1][:, i, :] for i in range(2)]
    silu_sb, h_sb = w_raw[1][:, 2, :], w_raw[1][:, 3, :]
    bank = [psum(st, f"bank{i}", [P, 512]) for i in range(5)]
    xt_ps = [psum(st, f"xt_ps{i}", [P, 512]) for i in range(2)]
    lg_ps = psum(st, "lg_ps", [P, TB, E])

    consts = sem("pj_consts")
    w_loaded = [sem(f"pj_w_loaded{i}") for i in range(2)]
    w_hi_done, w_lo_done = sem("pj_w_hi_done"), sem("pj_w_lo_done")
    x_loaded = [sem(f"pj_x_loaded{b}") for b in range(BATCH)]
    chain = sem("pj_chain")
    power_set = sem("pj_power_set")
    var_ready, rs_ready = sem("pj_var_ready"), sem("pj_rs_ready")
    xn_ready = sem("pj_xn_ready")
    id_done = sem("pj_id_done")
    xt_ready, xt_hi_done, xt_lo_done = sem("pj_xt_ready"), sem("pj_xt_hi_done"), sem("pj_xt_lo_done")
    lg_ready, lg_done = sem("pj_lg_ready"), sem("pj_lg_done")
    mm_done = sem("pj_mm_done")
    act_drained, dve_drained = sem("pj_act_drained"), sem("pj_dve_drained")
    rope_done = sem("pj_rope_done")
    rot_done, rot_hi_done, rot_lo_done = sem("pj_rot_done"), sem("pj_rot_hi_done"), sem("pj_rot_lo_done")
    rot_stored = [sem(f"pj_rot_stored{i}") for i in range(2)]
    v_set = sem("pj_v_set")
    v_stored = [sem(f"pj_v_stored{i}") for i in range(2)]
    h_hi_done, h_lo_done = sem("pj_h_hi_done"), sem("pj_h_lo_done")
    y_stored = [sem(f"pj_y_stored{i}") for i in range(2)]

    groups = []
    for m in (0, 1):
        for g in range(2):
            groups += [("qk", m, g, 0), ("qk", m, g, 1)]
    groups += [("v", t) for t in range(TB)]
    for i in range(KC):
        groups += [("gate", i), ("up", i)]
    groups += [("down", t) for t in range(TB)]
    NG = len(groups)
    NB = len(bank)

    def drained_by_act(k):
        return k[0] in ("qk", "gate", "down")

    order = [(b, g) for b in range(BATCH) for g in groups]

    def drains(n, act):
        return sum(drained_by_act(g) == act for _, g in order[:n])

    def await_drained(eng, n):
        a = drained_by_act(order[n][1])
        eng.wait_ge(act_drained if a else dve_drained, drains(n + 1, a))

    def number(b, *g):
        return b * NG + groups.index(g)

    block = st.enter_context(nc.Block())

    @block.sync
    def _(sp):
        sp.dma_start(id_f[:, :], ident).then_inc(id_done, 16)
        sp.dma_start(xn[:, 0:TB, :], x_b[0]).then_inc(x_loaded[0], 16)
        for m in range(NM):
            if m >= 2:
                sp.wait_ge(w_hi_done, m - 1)
                sp.wait_ge(w_lo_done, m - 1)
            sp.dma_start(w_raw[m % 2][:, :, :], mats[m]).then_inc(w_loaded[m % 2], 16)
            if m == 0:
                sp.dma_start(rw_sb[:, :, :], rw).then_inc(consts, 16)
                sp.dma_start(cos_sb[:, :], cos).then_inc(consts, 16)
                sp.dma_start(sin_sb[:, :], sin).then_inc(consts, 16)
                sp.dma_start(bqk_sb[:, :, :], bqk).then_inc(consts, 16)
                sp.dma_start(bv_sb[:, :], bv.partition_broadcast(P)).then_inc(consts, 16)
            if 1 <= m < BATCH:
                sp.dma_start(xn[:, m * TB:(m + 1) * TB, :], x_b[m]).then_inc(x_loaded[m], 16)
        n_rot = 0
        for b in range(BATCH):
            for m in (0, 1):
                stack = (q_stack, k_stack)[m]
                for g in range(2):
                    for half in (0, 1):
                        sp.wait_ge(rot_hi_done, n_rot + 1)
                        sp.wait_ge(rot_lo_done, n_rot + 1)
                        heads = stack[b * HEADS + 8 * g:b * HEADS + 8 * g + 8]
                        for part in range(3):
                            src = rot_lo[half] if part == (1, 2)[m] else rot_hi[half]
                            r = part * DH + half * HALF
                            sp.dma_start(heads[:, r:r + HALF, :], src[:, :].bitcast(F32)).then_inc(rot_stored[half], 16)
                        n_rot += 1
            for t in range(TB):
                n = b * TB + t
                await_drained(sp, number(b, "v", t))
                for_heads = v_dram[b * HEADS:(b + 1) * HEADS, :, t, :].rearrange("h p c -> p h c")
                sp.dma_start(for_heads, v_sb[n % 2]).then_inc(v_stored[n % 2], 16)
            for t in range(TB):
                n = b * TB + t
                await_drained(sp, number(b, "down", t))
                sp.dma_start(shared_dram[n], y_sb[n % 2]).then_inc(y_stored[n % 2], 16)
        for i in range(2):
            sp.wait_ge(rot_stored[i], 16 * 3 * n_rot // 2)
            sp.wait_ge(v_stored[i], 16 * NBLK // 2)
            sp.wait_ge(y_stored[i], 16 * NBLK // 2)

    @block.gpsimd
    def _(pool):
        pool.memset(power[:, :], -0.5).then_inc(power_set, 1)
        pool.wait_ge(power_set, 1)
        for b in range(BATCH):
            pool.wait_ge(var_ready, b + 1)
            pool.tensor_tensor(rs[:, :], var[:, :], power[:, :], ALU.pow).then_inc(rs_ready, 1)
            if b == 0:
                pool.wait_ge(w_hi_done, NM - 1)
                pool.wait_ge(w_lo_done, NM - 1)
                for i in range(2):
                    pool.memset(v_sb[i], 1.0).then_inc(v_set, 1)

    @block.vector
    def _(dve):
        links = [0]

        def link(ins):
            links[0] += 1
            ins.then_inc(chain, 1)
            dve.wait_ge(chain, links[0])

        def layer_norm(b):
            dve.wait_ge(x_loaded[b], 16)
            for t in range(TB):
                last = dve.bn_stats(stats[:, t, :], xn[:, b * TB + t, :])
            link(last)
            for t in range(TB):
                last = dve.bn_aggr(mv[:, t, :], stats[:, t, :])
            link(last)
            dve.tensor_scalar(var[:, :], mv[:, :, 1], EPS, None, ALU.add).then_inc(var_ready, 1)
            dve.wait_ge(rs_ready, b + 1)
            link(dve.tensor_tensor(rt[:, :], rs[:, :], rs[:, :], ALU.mult))
            link(dve.tensor_tensor(rt[:, :], rt[:, :], var[:, :], ALU.mult))
            link(dve.tensor_scalar(rt[:, :], rt[:, :], -0.5, 1.5, ALU.mult, ALU.add))
            link(dve.tensor_tensor(rs[:, :], rs[:, :], rt[:, :], ALU.mult))
            for t in range(TB):
                blk = xn[:, b * TB + t, :]
                dve.tensor_scalar(blk, blk, mv[:, t, 0:1], rs[:, t:t + 1], ALU.subtract, ALU.mult)\
                   .then_inc(xn_ready, 1)

        def split_x(b):
            for c in range(KC):
                n = b * KC + c
                dve.wait_ge(xt_hi_done, n + 1)
                dve.tensor_tensor(xt_lo[:, c, :], xt_ps[n % 2][:, :], xt_hi[:, c, :].bitcast(F32), ALU.subtract)\
                   .then_inc(xt_lo_done, 1)

        def split_w(m):
            dve.wait_ge(w_hi_done, m + 1)
            dve.tensor_tensor(w_lo[m][:, :, :], w_raw[m % 2][:, :, :], w_hi[m][:, :, :].bitcast(F32), ALU.subtract)\
               .then_inc(w_lo_done, 1)

        layer_norm(0)
        split_w(0)
        split_x(0)
        for m in range(1, NM):
            split_w(m)
        dve.wait_ge(consts, 80)
        dve.wait_ge(v_set, 2)
        n_rot = 0
        for b in range(BATCH):
            for m in (0, 1):
                for g in range(2):
                    await_drained(dve, number(b, "qk", m, g, 1))
                    x1, x2 = half_sb[0][:, :], half_sb[1][:, :]
                    t1, t2, t3 = (t[:, :] for t in rope_t)
                    if n_rot:
                        dve.wait_ge(rot_hi_done, n_rot)
                        dve.wait_ge(rot_lo_done, n_rot)
                    for to, h, table in ((t1, x1, cos_sb), (t2, x2, sin_sb), (t3, x2, cos_sb), (x1, x1, sin_sb)):
                        dve.tensor_tensor(to, h, table[:, :], ALU.mult).then_inc(rope_done, 1)
                    dve.wait_ge(rope_done, 4 * (4 * b + 2 * m + g + 1))
                    dve.tensor_tensor(t1, t1, t2, ALU.subtract).then_inc(rot_done, 1)
                    dve.tensor_tensor(t3, t3, x1, ALU.add).then_inc(rot_done, 1)
                    for half in (0, 1):
                        dve.wait_ge(rot_hi_done, n_rot + 1)
                        dve.tensor_tensor(rot_lo[half][:, :], rot[half][:, :], rot_hi[half][:, :].bitcast(F32),
                                          ALU.subtract).then_inc(rot_lo_done, 1)
                        n_rot += 1
            for t in range(TB):
                n = b * TB + t
                g = b * NG + groups.index(("v", t))
                dve.wait_ge(mm_done, g + 1)
                if n >= 2:
                    dve.wait_ge(v_stored[n % 2], 16 * (n // 2))
                dve.tensor_tensor(v_sb[n % 2][:, :, 0:DH], bank[g % NB][:, :].rearrange("p (h d) -> p h d", h=HEADS),
                                  bv_sb[:, :].rearrange("p (h d) -> p h d", h=HEADS), ALU.add).then_inc(dve_drained, 1)
            dve.wait_ge(lg_ready, b + 1)
            dve.tensor_copy(logits[:, b * TB:(b + 1) * TB, :], lg_ps[:, :, :]).then_inc(lg_done, 1)
            if b + 1 < BATCH:
                layer_norm(b + 1)
            for i in range(KC):
                n = b * KC + i
                g = b * NG + groups.index(("up", i))
                await_drained(dve, number(b, "gate", i))
                dve.wait_ge(mm_done, g + 1)
                if n:
                    dve.wait_ge(h_hi_done, n)
                    dve.wait_ge(h_lo_done, n)
                dve.tensor_tensor(h_sb, bank[g % NB][:, :], silu_sb, ALU.mult).then_inc(dve_drained, 1)
                dve.wait_ge(h_hi_done, n + 1)
                dve.tensor_tensor(ht_lo[:, i, :], h_sb, ht_hi[:, i, :].bitcast(F32), ALU.subtract)\
                   .then_inc(h_lo_done, 1)
            if b + 1 < BATCH:
                split_x(b + 1)

    @block.scalar
    def _(act):
        def split_w(m):
            act.wait_ge(w_loaded[m % 2], 16 * (m // 2 + 1))
            act.activation(w_hi[m][:, :, :], w_raw[m % 2][:, :, :], ACT.Copy).then_inc(w_hi_done, 1)

        def split_x(b, c):
            n = b * KC + c
            act.wait_ge(xt_ready, n + 1)
            if b and not c:
                act.wait_ge(lg_ready, b)
                act.wait_ge(mm_done, number(b - 1, "up", KC - 1) + 1)
            act.activation(xt_hi[:, c, :], xt_ps[n % 2][:, :], ACT.Copy).then_inc(xt_hi_done, 1)

        act.wait_ge(id_done, 16)
        act.activation(id_r[:, :], id_f[:, :], ACT.Copy).then_inc(id_done, 1)
        split_w(0)
        for c in range(KC):
            split_x(0, c)
        for m in range(1, NM):
            split_w(m)
        act.wait_ge(consts, 80)
        n_rot = 0
        for b in range(BATCH):
            for m in (0, 1):
                for g in range(2):
                    n = 4 * b + 2 * m + g
                    for half in (0, 1):
                        k = b * NG + groups.index(("qk", m, g, half))
                        act.wait_ge(mm_done, k + 1)
                        if n and not half:
                            act.wait_ge(rot_done, 2 * n)
                        act.activation(half_sb[half][:, :], bank[k % NB][:, :], ACT.Identity,
                                       bias=bqk_sb[:, m, 2 * g + half:2 * g + half + 1])\
                           .then_inc(act_drained, 1)
                    for half in (0, 1):
                        act.wait_ge(rot_done, n_rot + 1)
                        if n:
                            act.wait_ge(rot_stored[half], 16 * 3 * n)
                        act.activation(rot_hi[half][:, :], rot[half][:, :], ACT.Copy).then_inc(rot_hi_done, 1)
                        n_rot += 1
            for i in range(KC):
                n = b * KC + i
                k = b * NG + groups.index(("gate", i))
                act.wait_ge(mm_done, k + 1)
                if n == 0:
                    act.wait_ge(w_lo_done, NM)
                act.activation(silu_sb, bank[k % NB][:, :], ACT.Silu).then_inc(act_drained, 1)
                await_drained(act, number(b, "up", i))
                act.activation(ht_hi[:, i, :], h_sb, ACT.Copy).then_inc(h_hi_done, 1)
            for t in range(TB):
                if b + 1 < BATCH:
                    split_x(b + 1, t)
                n = b * TB + t
                k = b * NG + groups.index(("down", t))
                act.wait_ge(mm_done, k + 1)
                if n >= 2:
                    act.wait_ge(y_stored[n % 2], 16 * (n // 2))
                act.activation(y_sb[n % 2], bank[k % NB][:, :], ACT.Copy).then_inc(act_drained, 1)

    @block.tensor
    def _(pe):
        def transpose_x(b, c):
            n = b * KC + c
            if n >= 2:
                pe.wait_ge(xt_hi_done, n - 1)
                pe.wait_ge(xt_lo_done, n - 1)
            for t in range(TB):
                if c == 0:
                    pe.wait_ge(xn_ready, b * TB + t + 1)
                last = pe.transpose(xt_ps[n % 2][:, t * P:(t + 1) * P], xn[:, b * TB + t, c * P:(c + 1) * P], id_f[:, :])
            last.then_inc(xt_ready, 1)

        def three(bank_ap, pairs, k0, k1):
            for k, (a_hi, a_lo, b_hi, b_lo) in enumerate(pairs):
                pe.matmul(bank_ap, a_hi, b_hi, start=(k == 0 and k0), stop=False)
                pe.matmul(bank_ap, a_lo, b_hi, start=False, stop=False)
                last = pe.matmul(bank_ap, a_hi, b_lo, start=False, stop=(k == len(pairs) - 1 and k1))
            return last

        pe.wait_ge(id_done, 17)
        for c in range(KC):
            transpose_x(0, c)
        n = 0
        for b in range(BATCH):
            pe.wait_ge(xt_hi_done, (b + 1) * KC)
            pe.wait_ge(xt_lo_done, (b + 1) * KC)
            for g in groups:
                if n >= NB:
                    await_drained(pe, n - NB)
                to = bank[n % NB][:, :]
                if b == 0:
                    need = {"qk": WQ + g[1] + 1, "v": WV + 1, "gate": WG + 1, "up": WU + 1, "down": WD + 1}[g[0]]
                    pe.wait_ge(w_hi_done, need)
                    pe.wait_ge(w_lo_done, need)
                if g[0] == "qk":
                    c0 = (2 * g[2] + g[3]) * P
                    w = WQ + g[1]
                    last = three(to, [(w_hi[w][:, c, c0:c0 + P], w_lo[w][:, c, c0:c0 + P], xt_hi[:, c, :], xt_lo[:, c, :])
                                      for c in range(KC)], True, True)
                elif g[0] == "v":
                    t0 = g[1] * P
                    last = three(to, [(xt_hi[:, c, t0:t0 + P], xt_lo[:, c, t0:t0 + P], w_hi[WV][:, c, :], w_lo[WV][:, c, :])
                                      for c in range(KC)], True, True)
                elif g[0] in ("gate", "up"):
                    w = WG if g[0] == "gate" else WU
                    i0 = g[1] * P
                    last = three(to, [(w_hi[w][:, c, i0:i0 + P], w_lo[w][:, c, i0:i0 + P], xt_hi[:, c, :], xt_lo[:, c, :])
                                      for c in range(KC)], True, True)
                else:
                    if b + 1 < BATCH:
                        transpose_x(b + 1, g[1])
                    if g[1] == 0:
                        pe.wait_ge(h_hi_done, (b + 1) * KC)
                        pe.wait_ge(h_lo_done, (b + 1) * KC)
                    t0 = g[1] * P
                    last = three(to, [(ht_hi[:, i, t0:t0 + P], ht_lo[:, i, t0:t0 + P], w_hi[WD][:, i, :], w_lo[WD][:, i, :])
                                      for i in range(KC)], True, True)
                last.then_inc(mm_done, 1)
                n += 1
                if g == ("v", TB - 1):
                    pe.wait_ge(consts, 80)
                    if b:
                        pe.wait_ge(lg_done, b)
                    for t in range(TB):
                        for c in range(KC):
                            xs_ = xt_hi[:, c, t * P:(t + 1) * P].bitcast(F32)
                            xl_ = xt_lo[:, c, t * P:(t + 1) * P].bitcast(F32)
                            pe.matmul(lg_ps[:, t, :], xs_, rw_sb[:, c, :], start=(c == 0), stop=False)
                            last = pe.matmul(lg_ps[:, t, :], xl_, rw_sb[:, c, :], start=False, stop=(c == KC - 1))
                    last.then_inc(lg_ready, 1)


def route_stage(nc, st, sbuf, psum, logits, rbias, before_tok, before_e, before_g,
                iota_p, iota_t, iota_e, slot8, weight8, pad_slot, tile_slot, tile_need, ring_need):
    def sem(name):
        return st.enter_context(nc.semaphore(name))

    def tile(name, *shape, dt=F32):
        return sbuf(st, name, list(shape), dt)

    bias_sb = tile("bias_sb", P, E)
    before_tok_sb = tile("before_tok_sb", P, P)
    ones_sb = tile("ones_sb", P, P)
    before_e_sb = tile("before_e_sb", P, E, E)
    before_g_sb = tile("before_g_sb", P, GROUPS, GROUPS)
    iota_p_sb = tile("iota_p_sb", P, 1)
    iota_t_sb = tile("iota_t_sb", 1, TILES)
    iota_e_sb = tile("iota_e_sb", P, E)
    score = tile("score", P, NBLK, E)
    biased = tile("biased", P, NBLK, E)
    pair = [tile(f"pair{i}", P, NBLK * GROUPS) for i in range(7)]
    gscore = tile("gscore", P, NBLK, GROUPS)
    gbeats = tile("gbeats", P, NBLK, GROUPS, GROUPS)
    gties = tile("gties", P, NBLK, GROUPS, GROUPS)
    grank = tile("grank", P, NBLK, GROUPS)
    masked = tile("masked", P, NBLK, E)
    top8 = tile("top8", P, NBLK, TOPK)
    marked = tile("marked", P, NBLK, E)
    chosen = tile("chosen", P, NBLK, E)
    weight = tile("weight", P, NBLK, E)
    wsum = tile("wsum", P, NBLK)
    wrec = tile("wrec", P, NBLK)
    carry = tile("carry", P, NBLK + 1, E)
    padded_i = tile("padded_i", P, E, dt=I32)
    ntile = tile("ntile", P, E)
    ee = tile("ee", P, E, E)
    base = tile("base", P, E)
    pads = tile("pads", P, E)
    pads_before = tile("pads_before", P, E)
    slot = tile("slot", P, NBLK, E)
    slot8_f = tile("slot8_f", P, NBLK, TOPK)
    match = tile("match", P, NBLK, TOPK, E)
    small = [tile(f"small{i}", P, E) for i in range(6)]
    te = tile("te", 1, TILES, E)
    tile_e = tile("tile_e", 1, TILES)
    tile_ei = tile("tile_ei", 1, TILES, dt=I32)
    prefix_ps = psum(st, "prefix_ps", [P, NBLK, E])
    total_ps = psum(st, "total_ps", [P, NBLK, E])

    loaded, ones_set, score_done, chain = sem("rt_loaded"), sem("rt_ones_set"), sem("rt_score_done"), sem("rt_chain")
    chosen_ready, counted = sem("rt_chosen_ready"), sem("rt_counted")
    block = st.enter_context(nc.Block())

    @block.sync
    def _(sp):
        sp.dma_start(bias_sb[:, :], rbias.partition_broadcast(P)).then_inc(loaded, 16)
        for dst, src in ((before_tok_sb, before_tok), (iota_p_sb, iota_p), (iota_t_sb, iota_t)):
            sp.dma_start(dst[:, :], src).then_inc(loaded, 16)
        sp.dma_start(iota_e_sb[:, :], iota_e.partition_broadcast(P)).then_inc(loaded, 16)
        sp.dma_start(before_e_sb[:, :, :], before_e.partition_broadcast(P)).then_inc(loaded, 16)
        sp.dma_start(before_g_sb[:, :, :], before_g.partition_broadcast(P)).then_inc(loaded, 16)

    @block.gpsimd
    def _(pool):
        pool.memset(ones_sb[:, :], 1.0).then_inc(ones_set, 1)

    @block.scalar
    def _(act):
        act.activation(score[:, :, :], logits[:, :, :], ACT.Sigmoid).then_inc(score_done, 1)

    @block.tensor
    def _(pe):
        pe.wait_ge(ones_set, 1)
        pe.wait_ge(loaded, 112)
        pe.wait_ge(chosen_ready, 1)
        pe.matmul(prefix_ps[:, :, :], before_tok_sb[:, :], chosen[:, :, :], start=True, stop=True)
        pe.matmul(total_ps[:, :, :], ones_sb[:, :], chosen[:, :, :], start=True, stop=True).then_inc(counted, 1)

    @block.vector
    def _(dve):
        links = [0]

        def link(ins):
            links[0] += 1
            ins.then_inc(chain, 1)
            dve.wait_ge(chain, links[0])

        def tt(o, a, b, op):
            link(dve.tensor_tensor(o, a, b, op))

        def over_blocks(ap):
            return ap.unsqueeze(1).to_broadcast([P, NBLK, E])

        dve.wait_ge(loaded, 112)
        dve.wait_ge(score_done, 1)
        tt(biased[:, :, :], score[:, :, :], over_blocks(bias_sb[:, :]), ALU.add)

        four = biased[:, :, :].rearrange("p t (g c) -> p (t g) c", c=EPG)
        a, b, c, d = (four[:, :, i] for i in range(EPG))
        hi1, lo1, hi2, lo2, m1, t1, t2 = (x[:, :] for x in pair)
        dve.tensor_tensor(hi1, a, b, ALU.max)
        dve.tensor_tensor(lo1, a, b, ALU.min)
        dve.tensor_tensor(hi2, c, d, ALU.max)
        tt(lo2, c, d, ALU.min)
        dve.tensor_tensor(m1, hi1, hi2, ALU.max)
        dve.tensor_tensor(t1, hi1, hi2, ALU.min)
        tt(t2, lo1, lo2, ALU.max)
        tt(t1, t1, t2, ALU.max)
        tt(gscore[:, :, :].rearrange("p t g -> p (t g)"), m1, t1, ALU.add)

        mine = gscore[:, :, :].unsqueeze(3).to_broadcast([P, NBLK, GROUPS, GROUPS])
        other = gscore[:, :, :].unsqueeze(2).to_broadcast([P, NBLK, GROUPS, GROUPS])
        dve.tensor_tensor(gbeats[:, :, :, :], other, mine, ALU.is_gt)
        tt(gties[:, :, :, :], other, mine, ALU.is_equal)
        tt(gties[:, :, :, :], gties[:, :, :, :],
           before_g_sb[:, :, :].unsqueeze(1).to_broadcast([P, NBLK, GROUPS, GROUPS]), ALU.mult)
        tt(gbeats[:, :, :, :], gbeats[:, :, :, :], gties[:, :, :, :], ALU.add)
        link(dve.tensor_reduce(grank[:, :, :], gbeats[:, :, :, :], AX.X, ALU.add))
        link(dve.tensor_scalar(grank[:, :, :], grank[:, :, :], float(GSEL), None, ALU.is_lt))
        groups_of = masked[:, :, :].rearrange("p t (g c) -> p (t g) c", c=EPG)
        kept = grank[:, :, :].rearrange("p t g -> p (t g)").unsqueeze(2).to_broadcast([P, NBLK * GROUPS, EPG])
        tt(groups_of, four, kept, ALU.mult)

        for t in range(NBLK):
            last = dve.max(top8[:, t, :], masked[:, t, :])
        link(last)
        for t in range(NBLK):
            last = dve.match_replace(marked[:, t, :], top8[:, t, :], masked[:, t, :], NONE)
        link(last)
        dve.tensor_tensor(chosen[:, :, :], marked[:, :, :], masked[:, :, :], ALU.not_equal).then_inc(chosen_ready, 1)
        dve.wait_ge(chosen_ready, 1)
        tt(weight[:, :, :], score[:, :, :], chosen[:, :, :], ALU.mult)
        link(dve.tensor_reduce(wsum[:, :], weight[:, :, :], AX.X, ALU.add))
        link(dve.reciprocal(wrec[:, :], wsum[:, :]))
        link(dve.tensor_scalar(wrec[:, :], wrec[:, :], ROUTED_SCALE, None, ALU.mult))
        link(dve.tensor_tensor(weight[:, :, :], weight[:, :, :],
                               wrec[:, :].unsqueeze(2).to_broadcast([P, NBLK, E]), ALU.mult))

        dve.wait_ge(counted, 1)
        link(dve.memset(carry[:, 0, :], 0.0))
        for t in range(NBLK):
            tt(carry[:, t + 1, :], carry[:, t, :], total_ps[:, t, :], ALU.add)
        count = carry[:, NBLK, :]
        link(dve.tensor_scalar(padded_i[:, :], count, float(P - 1), None, ALU.add))
        link(dve.tensor_scalar(padded_i[:, :], padded_i[:, :], 7, None, ALU.logical_shift_right))
        link(dve.tensor_copy(ntile[:, :], padded_i[:, :]))
        link(dve.tensor_scalar(ntile[:, :], ntile[:, :], 1.0, None, ALU.max))

        def sum_before(o, v):
            tt(ee[:, :, :], before_e_sb[:, :, :], v.unsqueeze(1).to_broadcast([P, E, E]), ALU.mult)
            link(dve.tensor_reduce(o, ee[:, :, :], AX.X, ALU.add))

        sum_before(base[:, :], ntile[:, :])

        tt(slot[:, :, :], carry[:, 0:NBLK, :], prefix_ps[:, :, :], ALU.add)
        link(dve.tensor_scalar(small[0][:, :], base[:, :], float(P), None, ALU.mult))
        tt(slot[:, :, :], slot[:, :, :], over_blocks(small[0][:, :]), ALU.add)
        link(dve.scalar_tensor_tensor(out=slot[:, :, :], in0=slot[:, :, :], scalar=1.0, in1=chosen[:, :, :],
                                      op0=ALU.add, op1=ALU.mult))
        for t in range(NBLK):
            last = dve.max(slot8_f[:, t, :], slot[:, t, :])
        link(last)
        dve.tensor_scalar(slot8[:, :, :], slot8_f[:, :, :], -1.0, None, ALU.add)
        tt(match[:, :, :, :], slot[:, :, :].unsqueeze(2).to_broadcast([P, NBLK, TOPK, E]),
           slot8_f[:, :, :].unsqueeze(3).to_broadcast([P, NBLK, TOPK, E]), ALU.is_equal)
        tt(match[:, :, :, :], match[:, :, :, :],
           weight[:, :, :].unsqueeze(2).to_broadcast([P, NBLK, TOPK, E]), ALU.mult)
        dve.tensor_reduce(weight8[:, :, :], match[:, :, :, :], AX.X, ALU.add)

        link(dve.scalar_tensor_tensor(out=pads[:, :], in0=ntile[:, :], scalar=float(P), in1=count,
                                      op0=ALU.mult, op1=ALU.subtract))
        sum_before(pads_before[:, :], pads[:, :])
        in_tile, at, behind = small[1][:, :], small[2][:, :], small[3][:, :]
        dve.tensor_scalar(in_tile, pads[:, :], iota_p_sb[:, 0:1], None, ALU.is_gt)
        tt(at, small[0][:, :], count, ALU.add)
        link(dve.tensor_scalar(at, at, iota_p_sb[:, 0:1], None, ALU.add))
        tt(behind, iota_e_sb[:, :], pads_before[:, :], ALU.subtract)
        tt(behind, behind, pads[:, :], ALU.subtract)
        link(dve.tensor_scalar(behind, behind, iota_p_sb[:, 0:1], None, ALU.add))
        tt(small[4][:, 0:1], base[:, E - 1:E], ntile[:, E - 1:E], ALU.add)
        link(dve.tensor_scalar(small[4][:, 0:1], small[4][:, 0:1], float(P), None, ALU.mult))
        link(dve.tensor_scalar(behind, behind, small[4][:, 0:1], None, ALU.add))
        tt(at, at, behind, ALU.subtract)
        tt(at, at, in_tile, ALU.mult)
        tt(at, at, behind, ALU.add)
        dve.tensor_copy(pad_slot[:, :], at)

        tt(te[:, :, :], base[0:1, :].unsqueeze(1).to_broadcast([1, TILES, E]),
           iota_t_sb[:, :].unsqueeze(2).to_broadcast([1, TILES, E]), ALU.is_le)
        link(dve.tensor_reduce(tile_e[:, :], te[:, :, :], AX.X, ALU.add))
        dve.tensor_copy(tile_need[:, :], tile_e[:, :])
        link(dve.tensor_scalar(tile_ei[:, :], tile_e[:, :], -1.0, None, ALU.add))
        dve.tensor_scalar(tile_slot[:, :], tile_ei[:, :], WRING - 1, None, ALU.bitwise_and)
        link(dve.memset(small[5][0:1, :], 1.0))
        link(dve.tensor_scalar(small[5][0:1, WRING:E], base[0:1, 1:E - WRING + 1], 1.0, None, ALU.add))
        link(dve.tensor_copy(ring_need[:, :], small[5][0:1, :]))


def attend_stage(nc, st, sbuf, psum, q_stack, k_stack, v_dram, wo, bo, attn_dram, id_r,
                 xn, slot8, pad_slot, xs_dram, spread):
    def sem(name):
        return st.enter_context(nc.semaphore(name))

    QUAD = P // DH
    NQ = HEADS // QUAD
    QB = SEQ // P
    NH = BATCH * HEADS
    wo_raw = sbuf(st, "wo_raw", [P, KC, D])
    wo_hi = sbuf(st, "wo_hi", [P, KC, D], F32R)
    wo_lo = sbuf(st, "wo_lo", [P, KC, D], F32R)
    bo_sb = sbuf(st, "bo_sb", [P, D])
    ones = sbuf(st, "ones", [P, SEQ])
    zeros = sbuf(st, "zeros", [P, D])
    q_sb = [sbuf(st, f"q_sb{i}", [P, SEQ], F32R) for i in range(QUAD)]
    k_sb = [sbuf(st, f"k_sb{i}", [P, SEQ], F32R) for i in range(QUAD)]
    v_sb = [sbuf(st, f"va_sb{i}", [P, QB, VW]) for i in range(QUAD)]
    row_max = sbuf(st, "row_max", [P, QB])
    neg_max = sbuf(st, "neg_max", [P, QB, 2], F32R)
    prob = [sbuf(st, f"prob{i}", [P, QB, SEQ]) for i in range(2)]
    recip = sbuf(st, "recip", [DH, SEQ])
    o_sb = sbuf(st, "o_sb", [P, NQ, SEQ])
    o_hi = sbuf(st, "o_hi", [P, NQ, SEQ], F32R)
    o_lo = sbuf(st, "o_lo", [P, NQ, SEQ], F32R)
    y_sb = [sbuf(st, f"ya_sb{i}", [P, D]) for i in range(2)]
    s_ps = [psum(st, f"s_ps{i}", [P, SEQ]) for i in range(2)]
    st_ps = [psum(st, f"st_ps{i}", [P, SEQ]) for i in range(2)]
    o_ps = [psum(st, f"o_ps{i}", [P, SEQ]) for i in range(2)]
    m_ps = psum(st, "m_ps", [2, SEQ], F32R)
    y_ps = psum(st, "y_ps", [P, D])

    wo_loaded, wo_hi_done, wo_lo_done = sem("at_wo_loaded"), sem("at_wo_hi_done"), sem("at_wo_lo_done")
    bo_loaded, ones_set, k_ones = sem("at_bo_loaded"), sem("at_ones_set"), sem("at_k_ones")
    zeros_set = sem("at_zeros_set")
    head_in = [sem(f"at_head_in{i}") for i in range(QUAD)]
    s_ready, neg_hi, neg_done = sem("at_s_ready"), sem("at_neg_hi"), sem("at_neg_done")
    m_ready, m_rows = sem("at_m_ready"), sem("at_m_rows")
    st_ready, rec_done = sem("at_st_ready"), sem("at_rec_done")
    o_hi_done, o_lo_done = sem("at_o_hi_done"), sem("at_o_lo_done")
    y_ready = sem("at_y_ready")
    max_done, MAX0 = sem("at_max_done"), 2
    exp_done, EXP0 = sem("at_exp_done"), 2
    head_done, HEAD0 = sem("at_head_done"), 2
    o_done, O0 = sem("at_o_done"), QUAD
    y_done, Y0 = sem("at_y_done"), 1
    y_stored = [sem(f"at_y_stored{i}") for i in range(2)]
    STORED0 = 16

    def walk(eng, quad, project):
        with eng.Fori(0, BATCH - 1) as b:
            with eng.Fori(0, NQ) as c:
                quad(b, c, False)
            project(b)
        with eng.Fori(0, NQ - 1) as c:
            quad(BATCH - 1, c, False)
        quad(BATCH - 1, NQ - 1, True)
        project(BATCH - 1)

    def following(g, i):
        return (g, i + 1) if i + 1 < QUAD else (g + 1, 0)

    block = st.enter_context(nc.Block())

    @block.sync
    def _(sp):
        sp.dma_start(wo_raw[:, :, :], wo).then_inc(wo_loaded, 16)
        sp.dma_start(bo_sb[:, :], bo.partition_broadcast(P)).then_inc(bo_loaded, 16)

        def load(g, i):
            n = g * QUAD + i
            one = slice(n, n + 1) if isinstance(n, int) else bass.ds(n, 1)
            sp.dma_start(q_sb[i][0:STACK, :].bitcast(F32), q_stack[one].rearrange("a r s -> (a r) s")).then_inc(head_in[i], 16)
            sp.dma_start(k_sb[i][0:STACK, :].bitcast(F32), k_stack[one].rearrange("a r s -> (a r) s")).then_inc(head_in[i], 16)
            sp.dma_start(v_sb[i][:, :, :], v_dram[one].rearrange("a p t c -> (a p) t c")).then_inc(head_in[i], 16)

        for i in range(QUAD):
            load(0, i)

        def quad(b, c, final):
            g = b * NQ + c
            if not final:
                for i in range(QUAD):
                    sp.wait_ge(head_done, g * QUAD + (i + 1 + HEAD0))
                    load(g + 1, i)

        def project(b):
            for t in range(TB):
                sp.wait_ge(y_done, b * TB + (t + 1 + Y0))
                n = b * TB + t
                one = slice(n, n + 1) if isinstance(n, int) else bass.ds(n, 1)
                sp.dma_start(attn_dram[one].rearrange("a p d -> (a p) d"), y_sb[t % 2][:, :]).then_inc(y_stored[t % 2], 16)

        walk(sp, quad, project)
        for i in range(2):
            sp.wait_ge(y_stored[i], STORED0 + 16 * NBLK // 2)

    @block.gpsimd
    def _(pool):
        pool.memset(ones[:, :], 1.0).then_inc(ones_set, 1)
        pool.memset(zeros[:, :], 0.0).then_inc(zeros_set, 1)
        pool.wait_ge(zeros_set, 1)
        for t in range(NBLK):
            for k in range(TOPK):
                pool.indirect_dma_start(xs_dram, bass.IndirectOffsetOnAxis(slot8[:, t, k:k + 1], 0), xn[:, t, :], None,
                                        bounds_check=SLOTS - 1, oob_is_err=False).then_inc(spread, 16)
        for e in range(E):
            pool.indirect_dma_start(xs_dram, bass.IndirectOffsetOnAxis(pad_slot[:, e:e + 1], 0), zeros[:, :], None,
                                    bounds_check=SLOTS - 1, oob_is_err=False).then_inc(spread, 16)
        pool.wait_ge(spread, 16 * (NBLK * TOPK + E))

    @block.tensor
    def _(pe):
        pe.sem_inc(head_done, HEAD0)
        pe.wait_ge(k_ones, QUAD)

        def scores(g, i, qb):
            if qb == 0:
                pe.wait_ge(head_in[i], g * 48 + 48)
            pe.wait_ge(max_done, g * (QUAD * QB) + (i * QB + qb - 1 + MAX0))
            pe.matmul(s_ps[qb % 2][:, :], q_sb[i][0:STACK, qb * P:(qb + 1) * P], k_sb[i][0:STACK, :],
                      start=True, stop=True).then_inc(s_ready, 1)

        def max_rows(g, i):
            pe.wait_ge(neg_done, g * QUAD + (i + 1))
            for qb in range(QB):
                last = pe.transpose(m_ps[:, qb * P:(qb + 1) * P], neg_max[:, qb, :], id_r[:, :])
            last.then_inc(m_ready, 1)

        for qb in range(QB):
            scores(0, 0, qb)
        max_rows(0, 0)

        def quad(b, c, final):
            g = b * NQ + c
            for i in range(QUAD):
                more = not (final and i == QUAD - 1)
                g1, i1 = following(g, i)
                o = o_ps[i // 2][VW * (i % 2):VW * (i % 2) + VW, :]

                def shifted(kb):
                    if kb == 0:
                        pe.wait_ge(m_rows, g * QUAD + (i + 1))
                    pe.wait_ge(exp_done, g * (QUAD * QB) + (i * QB + kb - 1 + EXP0))
                    pe.matmul(st_ps[kb % 2][:, :], k_sb[i][0:STACK + 2, kb * P:(kb + 1) * P], q_sb[i][0:STACK + 2, :],
                              start=True, stop=True).then_inc(st_ready, 1)

                def outputs(kb):
                    if kb == 0:
                        pe.wait_ge(o_done, g * QUAD + (i + 1 - QUAD + O0))
                    pe.wait_ge(exp_done, g * (QUAD * QB) + (i * QB + kb + 1 + EXP0))
                    mm = pe.matmul(o, v_sb[i][:, kb, :], prob[i % 2][:, kb, :], start=(kb == 0), stop=(kb == QB - 1))
                    if kb == QB - 1:
                        mm.then_inc(head_done, 1)

                for kb in range(QB):
                    shifted(kb)
                    if more:
                        scores(g1, i1, kb)
                    if kb:
                        outputs(kb - 1)
                if more:
                    max_rows(g1, i1)
                outputs(QB - 1)

        def project(b):
            pe.wait_ge(wo_hi_done, 1)
            pe.wait_ge(wo_lo_done, 1)
            pe.wait_ge(o_hi_done, b + 1)
            pe.wait_ge(o_lo_done, b + 1)
            for t in range(TB):
                pe.wait_ge(y_done, b * TB + (t + Y0))
                for c in range(NQ):
                    a_hi, a_lo = o_hi[:, c, t * P:(t + 1) * P], o_lo[:, c, t * P:(t + 1) * P]
                    pe.matmul(y_ps[:, :], a_hi, wo_hi[:, c, :], start=(c == 0), stop=False)
                    pe.matmul(y_ps[:, :], a_lo, wo_hi[:, c, :], start=False, stop=False)
                    last = pe.matmul(y_ps[:, :], a_hi, wo_lo[:, c, :], start=False, stop=(c == NQ - 1))
                last.then_inc(y_ready, 1)

        walk(pe, quad, project)

    @block.scalar
    def _(act):
        act.sem_inc(exp_done, EXP0)
        act.wait_ge(wo_loaded, 16)
        act.activation(wo_hi[:, :, :], wo_raw[:, :, :], ACT.Copy).then_inc(wo_hi_done, 1)

        def rows(g, i):
            act.wait_ge(m_ready, g * QUAD + (i + 1))
            act.activation(q_sb[i][STACK:STACK + 2, :], m_ps[:, :].bitcast(F32), ACT.Copy).then_inc(m_rows, 1)

        rows(0, 0)

        def quad(b, c, final):
            g = b * NQ + c
            for i in range(QUAD):
                act.wait_ge(head_done, g * QUAD + (i - 1 + HEAD0))
                for kb in range(QB):
                    act.wait_ge(st_ready, g * (QUAD * QB) + (i * QB + kb + 1))
                    act.activation(prob[i % 2][:, kb, :], st_ps[kb % 2][:, :], ACT.Exp, scale=SCALE).then_inc(exp_done, 1)
                if not (final and i == QUAD - 1):
                    rows(*following(g, i))

        def project(b):
            act.wait_ge(o_done, b * HEADS + (HEADS + O0))
            act.activation(o_hi[:, :, :], o_sb[:, :, :], ACT.Copy).then_inc(o_hi_done, 1)

        walk(act, quad, project)

    @block.vector
    def _(dve):
        dve.sem_inc(max_done, MAX0)
        dve.sem_inc(o_done, O0)
        dve.sem_inc(y_done, Y0)
        for i in range(2):
            dve.sem_inc(y_stored[i], STORED0)
        dve.wait_ge(ones_set, 1)
        for i in range(QUAD):
            dve.tensor_copy(k_sb[i][STACK:STACK + 2, :], ones[STACK:STACK + 2, :]).then_inc(k_ones, 1)

        def maxima(g, i):
            for qb in range(QB):
                dve.wait_ge(s_ready, g * (QUAD * QB) + (i * QB + qb + 1))
                dve.tensor_reduce(row_max[:, qb:qb + 1], s_ps[qb % 2][:, :], AX.X, ALU.max).then_inc(max_done, 1)
            dve.wait_ge(max_done, g * (QUAD * QB) + ((i + 1) * QB + MAX0))
            dve.tensor_scalar(neg_max[:, :, 0], row_max[:, :], -1.0, None, ALU.mult).then_inc(neg_hi, 1)
            dve.wait_ge(neg_hi, g * QUAD + (i + 1))
            dve.scalar_tensor_tensor(out=neg_max[:, :, 1], in0=row_max[:, :], scalar=-1.0, in1=neg_max[:, :, 0].bitcast(F32),
                                     op0=ALU.mult, op1=ALU.subtract).then_inc(neg_done, 1)

        maxima(0, 0)
        dve.wait_ge(wo_hi_done, 1)
        dve.tensor_tensor(wo_lo[:, :, :], wo_raw[:, :, :], wo_hi[:, :, :].bitcast(F32), ALU.subtract).then_inc(wo_lo_done, 1)
        dve.wait_ge(bo_loaded, 16)

        def quad(b, c, final):
            g = b * NQ + c
            for i in range(QUAD):
                if not (final and i == QUAD - 1):
                    maxima(*following(g, i))
                r = VW * (i % 2)
                dve.wait_ge(head_done, g * QUAD + (i + 1 + HEAD0))
                dve.wait_ge(o_done, g * QUAD + (i + O0))
                dve.reciprocal(recip[:, :], o_ps[i // 2][r + DH:r + VW, :]).then_inc(rec_done, 1)
                dve.wait_ge(rec_done, g * QUAD + (i + 1))
                to = o_sb[DH * i:DH * (i + 1), c, :] if isinstance(c, int) else \
                    o_sb[DH * i:DH * (i + 1), bass.ds(c, 1), :].rearrange("p a s -> p (a s)")
                dve.tensor_tensor(to, o_ps[i // 2][r:r + DH, :], recip[:, :], ALU.mult).then_inc(o_done, 1)

        def project(b):
            dve.wait_ge(o_hi_done, b + 1)
            dve.tensor_tensor(o_lo[:, :, :], o_sb[:, :, :], o_hi[:, :, :].bitcast(F32), ALU.subtract).then_inc(o_lo_done, 1)
            for t in range(TB):
                dve.wait_ge(y_ready, b * TB + (t + 1))
                dve.wait_ge(y_stored[t % 2], b * 32 + (16 * (t // 2) + STORED0))
                dve.tensor_tensor(y_sb[t % 2][:, :], y_ps[:, :], bo_sb[:, :], ALU.add).then_inc(y_done, 1)

        walk(dve, quad, project)


def experts_stage(nc, st, sbuf, psum, xs_dram, ys_dram, wexp, id_f, id_r, tile_slot, tile_need, ring_need):
    def sem(name):
        return st.enter_context(nc.semaphore(name))

    GU = KC * 2 * INNER
    IC = INNER // P
    w_raw = [sbuf(st, f"we_raw{i}", [P, WCOLS]) for i in range(2)]
    w_hi = sbuf(st, "we_hi", [P, WRING, WCOLS], F32R)
    w_lo = sbuf(st, "we_lo", [P, WRING, WCOLS], F32R)
    zero = sbuf(st, "we_zero", [P, WCOLS])
    x_sb = [sbuf(st, f"xe_sb{i}", [P, D], F32R) for i in range(2)]
    xt_hi = [sbuf(st, f"xe_hi{i}", [P, KC, P], F32R) for i in range(2)]
    xt_lo = [sbuf(st, f"xe_lo{i}", [P, KC, P], F32R) for i in range(2)]
    silu_sb = sbuf(st, "silu_e", [P, INNER])
    h_sb = sbuf(st, "h_e", [P, INNER])
    ht_hi = sbuf(st, "ht_e_hi", [P, IC, P], F32R)
    ht_lo = sbuf(st, "ht_e_lo", [P, IC, P], F32R)
    y_sb = [sbuf(st, f"ye_sb{i}", [P, D]) for i in range(2)]
    xt_ps = psum(st, "xe_ps", [P, KC, P], F32R)
    gu_ps = [psum(st, f"gu_ps{i}", [P, 2 * INNER]) for i in range(2)]
    ht_ps = psum(st, "he_ps", [P, IC, P])
    y_ps = [psum(st, f"ye_ps{i}", [P, D]) for i in range(2)]

    raw_in = [sem(f"ex_raw_in{i}") for i in range(2)]
    zero_set, hi_done, w_ready = sem("ex_zero_set"), sem("ex_hi_done"), sem("ex_w_ready")
    x_in = [sem(f"ex_x_in{i}") for i in range(2)]
    xt_ready, xt_hi_done, xt_lo_done = sem("ex_xt_ready"), sem("ex_xt_hi_done"), sem("ex_xt_lo_done")
    gu_ready, silu_done, h_done = sem("ex_gu_ready"), sem("ex_silu_done"), sem("ex_h_done")
    ht_ready, ht_hi_done, ht_lo_done = sem("ex_ht_ready"), sem("ex_ht_hi_done"), sem("ex_ht_lo_done")
    y_copied, COPIED0 = sem("ex_y_copied"), 2
    y_stored, STORED0 = [sem(f"ex_y_stored{i}") for i in range(2)], 16
    tiles_done, TILES0 = sem("ex_tiles_done"), 1

    def walk(eng, step):
        step(0, 0, False, True)
        with eng.Fori(0, (TILES - 2) // 2) as turn:
            step(turn * 2 + 1, 1, True, True)
            step(turn * 2 + 2, 0, True, True)
        step(TILES - 1, 1, True, False)

    def rows(dram, t):
        return dram[t * P:(t + 1) * P, :] if isinstance(t, int) else dram[bass.ds(t * P, P), :]

    def half(t, p):
        return 16 * ((t - p) // 2) if isinstance(t, int) else (t - p) * 8

    block = st.enter_context(nc.Block())

    @block.sync
    def _(sp):
        for p in range(2):
            sp.dma_start(x_sb[p][:, :].bitcast(F32), rows(xs_dram, p)).then_inc(x_in[p], 16)

        def step(t, p, before, behind):
            if behind:
                sp.wait_ge(xt_ready, t + 1)
                if not isinstance(t, int) or t + 2 < TILES:
                    sp.dma_start(x_sb[p][:, :].bitcast(F32), rows(xs_dram, t + 2)).then_inc(x_in[p], 16)
            if before:
                sp.wait_ge(y_copied, t + COPIED0)
                sp.dma_start(rows(ys_dram, t - 1), y_sb[1 - p][:, :]).then_inc(y_stored[1 - p], 16)

        step(0, 0, False, True)
        with sp.Fori(0, (TILES - 4) // 2) as turn:
            step(turn * 2 + 1, 1, True, True)
            step(turn * 2 + 2, 0, True, True)
        for t in range(TILES - 3, TILES):
            step(t, t % 2, True, t < TILES - 1)
        sp.wait_ge(y_copied, TILES + COPIED0)
        sp.dma_start(rows(ys_dram, TILES - 1), y_sb[1][:, :]).then_inc(y_stored[1], 16)
        for p in range(2):
            sp.wait_ge(y_stored[p], 16 * TILES // 2 + STORED0)

    @block.gpsimd
    def _(pool):
        pool.memset(zero[:, :], 0.0).then_inc(zero_set, 1)
        for e in range(2):
            pool.dma_start(w_raw[e][:, :], wexp[e]).then_inc(raw_in[e], 16)
        pool.wait_ge(zero_set, 1)

        def split(e, r, more):
            if not isinstance(e, int) or e >= WRING:
                at = ring_need[0:1, e:e + 1] if isinstance(e, int) else ring_need[0:1, bass.ds(e, 1)]
                need = pool.value_load(at, min_val=1, max_val=TILES + 1)
                pool.wait_ge(tiles_done, need)
            raw = w_raw[r % 2]
            k = 16 * (e // 2 + 1) if isinstance(e, int) else (e - r % 2) * 8 + 16
            pool.wait_ge(raw_in[r % 2], k)
            pool.tensor_tensor(w_hi[:, r, :], raw[:, :], zero[:, :], ALU.add).then_inc(hi_done, 1)
            pool.wait_ge(hi_done, e + 1)
            pool.tensor_tensor(w_lo[:, r, :], raw[:, :], w_hi[:, r, :].bitcast(F32), ALU.subtract).then_inc(w_ready, 1)
            if more:
                pool.wait_ge(w_ready, e + 1)
                one = slice(e + 2, e + 3) if isinstance(e, int) else bass.ds(e + 2, 1)
                pool.dma_start(raw[:, :], wexp[one].rearrange("a p c -> (a p) c")).then_inc(raw_in[r % 2], 16)

        for e in range(WRING):
            split(e, e, True)
        with pool.Fori(1, E // WRING - 1) as turn:
            for r in range(WRING):
                split(turn * WRING + r, r, True)
        for r in range(WRING):
            split(E - WRING + r, r, r < WRING - 2)

    @block.tensor
    def _(pe):
        pe.sem_inc(tiles_done, TILES0)

        def place(t):
            at = tile_slot[0:1, t:t + 1] if isinstance(t, int) else tile_slot[0:1, bass.ds(t, 1)]
            r = pe.value_load(at, min_val=0, max_val=WRING - 1)
            return (w_hi[:, bass.ds(r, 1), :].rearrange("p a c -> p (a c)"),
                    w_lo[:, bass.ds(r, 1), :].rearrange("p a c -> p (a c)"))

        def transpose_x(t, p):
            pe.wait_ge(x_in[p], half(t, p) + 16)
            if not isinstance(t, int) or t:
                pe.wait_ge(xt_hi_done, t)
                pe.wait_ge(xt_lo_done, t)
            for c in range(KC):
                last = pe.transpose(xt_ps[:, c, :], x_sb[p][:, c * P:(c + 1) * P], id_r[:, :])
            last.then_inc(xt_ready, 1)

        def transpose_h(t):
            pe.wait_ge(h_done, t + 1)
            for c in range(IC):
                last = pe.transpose(ht_ps[:, c, :], h_sb[:, c * P:(c + 1) * P], id_f[:, :])
            last.then_inc(ht_ready, 1)

        def down(t, p):
            hi, lo = place(t)
            pe.wait_ge(ht_hi_done, t + 1)
            pe.wait_ge(ht_lo_done, t + 1)
            pe.wait_ge(y_copied, t - 1 + COPIED0)
            for c in range(IC):
                w = slice(GU + c * D, GU + (c + 1) * D)
                pe.matmul(y_ps[p][:, :], ht_hi[:, c, :], hi[:, w], start=(c == 0), stop=False)
                pe.matmul(y_ps[p][:, :], ht_lo[:, c, :], hi[:, w], start=False, stop=False)
                last = pe.matmul(y_ps[p][:, :], ht_hi[:, c, :], lo[:, w], start=False, stop=(c == IC - 1))
            last.then_inc(tiles_done, 1)

        def step(t, p, before, behind):
            if before:
                transpose_h(t - 1)
            if behind:
                transpose_x(t + 1, 1 - p)
            hi, lo = place(t)
            at = tile_need[0:1, t:t + 1] if isinstance(t, int) else tile_need[0:1, bass.ds(t, 1)]
            need = pe.value_load(at, min_val=1, max_val=E)
            pe.wait_ge(w_ready, need)
            pe.wait_ge(xt_hi_done, t + 1)
            pe.wait_ge(xt_lo_done, t + 1)
            for c in range(KC):
                w = slice(c * 2 * INNER, (c + 1) * 2 * INNER)
                pe.matmul(gu_ps[p][:, :], xt_hi[p][:, c, :], hi[:, w], start=(c == 0), stop=False)
                pe.matmul(gu_ps[p][:, :], xt_lo[p][:, c, :], hi[:, w], start=False, stop=False)
                last = pe.matmul(gu_ps[p][:, :], xt_hi[p][:, c, :], lo[:, w], start=False, stop=(c == KC - 1))
            last.then_inc(gu_ready, 1)
            if before:
                down(t - 1, 1 - p)

        transpose_x(0, 0)
        walk(pe, step)
        transpose_h(TILES - 1)
        down(TILES - 1, 1)

    @block.scalar
    def _(act):
        def x_hi(t, p):
            act.wait_ge(xt_ready, t + 1)
            act.activation(xt_hi[p][:, :, :], xt_ps[:, :, :].bitcast(F32), ACT.Copy).then_inc(xt_hi_done, 1)

        def h_hi(t):
            act.wait_ge(ht_ready, t + 1)
            act.activation(ht_hi[:, :, :], ht_ps[:, :, :], ACT.Copy).then_inc(ht_hi_done, 1)

        def y_copy(t, p):
            act.wait_ge(tiles_done, t + (1 + TILES0))
            act.wait_ge(y_stored[p], half(t, p) + STORED0)
            act.activation(y_sb[p][:, :], y_ps[p][:, :], ACT.Copy).then_inc(y_copied, 1)

        def step(t, p, before, behind):
            if before:
                h_hi(t - 1)
            if behind:
                x_hi(t + 1, 1 - p)
            act.wait_ge(gu_ready, t + 1)
            if before:
                act.wait_ge(h_done, t)
            act.activation(silu_sb[:, :], gu_ps[p][:, 0:INNER], ACT.Silu).then_inc(silu_done, 1)
            if before:
                y_copy(t - 1, 1 - p)

        act.sem_inc(y_copied, COPIED0)
        for p in range(2):
            act.sem_inc(y_stored[p], STORED0)
        x_hi(0, 0)
        walk(act, step)
        h_hi(TILES - 1)
        y_copy(TILES - 1, 1)

    @block.vector
    def _(dve):
        def x_lo(t, p):
            dve.wait_ge(xt_hi_done, t + 1)
            dve.tensor_tensor(xt_lo[p][:, :, :], xt_ps[:, :, :].bitcast(F32), xt_hi[p][:, :, :].bitcast(F32), ALU.subtract)\
               .then_inc(xt_lo_done, 1)

        def h_lo(t):
            dve.wait_ge(ht_hi_done, t + 1)
            dve.tensor_tensor(ht_lo[:, :, :], ht_ps[:, :, :], ht_hi[:, :, :].bitcast(F32), ALU.subtract).then_inc(ht_lo_done, 1)

        def step(t, p, before, behind):
            if before:
                h_lo(t - 1)
            if behind:
                x_lo(t + 1, 1 - p)
            dve.wait_ge(silu_done, t + 1)
            dve.tensor_tensor(h_sb[:, :], gu_ps[p][:, INNER:2 * INNER], silu_sb[:, :], ALU.mult).then_inc(h_done, 1)

        x_lo(0, 0)
        walk(dve, step)
        h_lo(TILES - 1)


def combine_stage(nc, st, sbuf, slot8, weight8, ys_dram, shared_dram, attn_dram, x_blk, out_b):
    def sem(name):
        return st.enter_context(nc.semaphore(name))

    rows = [[sbuf(st, f"rows{i}_{k}", [P, D]) for k in range(TOPK)] for i in range(2)]
    shared = [sbuf(st, f"shared{i}", [P, D]) for i in range(2)]
    attn = [sbuf(st, f"attn{i}", [P, D]) for i in range(2)]
    x_sb = [sbuf(st, f"x_sb{i}", [P, D]) for i in range(2)]
    acc = [sbuf(st, f"acc{i}", [P, D]) for i in range(2)]
    act_sb = [sbuf(st, f"act_sb{i}", [P, D]) for i in range(2)]
    o_sb = [sbuf(st, f"out_sb{i}", [P, D]) for i in range(2)]
    rows_in = [sem(f"cb_rows_in{i}") for i in range(2)]
    rest_in = [sem(f"cb_rest_in{i}") for i in range(2)]
    chain, sum_done, silu_done, out_done = sem("cb_chain"), sem("cb_sum_done"), sem("cb_silu_done"), sem("cb_out_done")
    stored = [sem(f"cb_stored{i}") for i in range(2)]
    block = st.enter_context(nc.Block())

    @block.gpsimd
    def _(pool):
        for t in range(NBLK):
            i = t % 2
            if t >= 2:
                pool.wait_ge(sum_done, t - 1)
            for k in range(TOPK):
                pool.indirect_dma_start(rows[i][k][:, :], None, ys_dram,
                                        bass.IndirectOffsetOnAxis(slot8[:, t, k:k + 1], 0),
                                        bounds_check=SLOTS - 1, oob_is_err=False).then_inc(rows_in[i], 16)

    @block.sync
    def _(sp):
        for t in range(NBLK):
            i = t % 2
            if t >= 2:
                sp.wait_ge(out_done, t - 1)
            sp.dma_start(shared[i][:, :], shared_dram[t]).then_inc(rest_in[i], 16)
            sp.dma_start(attn[i][:, :], attn_dram[t]).then_inc(rest_in[i], 16)
            sp.dma_start(x_sb[i][:, :], x_blk[t]).then_inc(rest_in[i], 16)
            if t:
                sp.wait_ge(out_done, t)
                sp.dma_start(out_b[t - 1], o_sb[1 - i][:, :]).then_inc(stored[1 - i], 16)
        sp.wait_ge(out_done, NBLK)
        sp.dma_start(out_b[NBLK - 1], o_sb[1][:, :]).then_inc(stored[1], 16)
        for i in range(2):
            sp.wait_ge(stored[i], 16 * NBLK // 2)

    @block.vector
    def _(dve):
        links = [0]

        def link(ins):
            links[0] += 1
            ins.then_inc(chain, 1)
            dve.wait_ge(chain, links[0])

        def finish(t):
            i = t % 2
            dve.wait_ge(silu_done, t + 1)
            link(dve.tensor_tensor(act_sb[i][:, :], act_sb[i][:, :], attn[i][:, :], ALU.mult))
            if t >= 2:
                dve.wait_ge(stored[i], 16 * (t // 2))
            dve.tensor_tensor(o_sb[i][:, :], act_sb[i][:, :], x_sb[i][:, :], ALU.add).then_inc(out_done, 1)

        for t in range(NBLK):
            i = t % 2
            dve.wait_ge(rest_in[i], 48 * (t // 2 + 1))
            dve.wait_ge(rows_in[i], 16 * TOPK * (t // 2 + 1))
            for k in range(TOPK):
                ins = dve.scalar_tensor_tensor(out=acc[i][:, :], in0=rows[i][k][:, :], scalar=weight8[:, t, k:k + 1],
                                               in1=acc[i][:, :] if k else shared[i][:, :], op0=ALU.mult, op1=ALU.add)
                if k < TOPK - 1:
                    link(ins)
                else:
                    ins.then_inc(sum_done, 1)
            if t:
                finish(t - 1)
        finish(NBLK - 1)

    @block.scalar
    def _(act):
        for t in range(NBLK):
            i = t % 2
            act.wait_ge(sum_done, t + 1)
            if t >= 2:
                act.wait_ge(out_done, t - 1)
            act.activation(act_sb[i][:, :], acc[i][:, :], ACT.Silu).then_inc(silu_done, 1)



def rope_tables():
    inv = (1.0 / np.float32(10000.0) ** (np.arange(0, DH, 2, dtype=np.float32) / np.float32(DH))).astype(np.float32)
    angle = np.arange(SEQ, dtype=np.float32)[None, :] * np.tile(inv, P // HALF)[:, None]
    return np.cos(angle).astype(np.float32), np.sin(angle).astype(np.float32)


def kernel(**inputs):
    import concourse.bacc as bacc
    from concourse.bass_utils import run_bass_kernel_spmd

    a = {k: np.asarray(v) for k, v in inputs.items()}

    def by_rows(w):
        return np.ascontiguousarray(w.reshape(-1, P, w.shape[-1]).transpose(1, 0, 2))

    perm = np.arange(D).reshape(2, 8, 2, HALF).transpose(0, 2, 1, 3).reshape(-1)
    wqk = np.stack([by_rows(a[f"L0_attn_{m}_w"][perm].T) for m in "qk"])
    bqk = np.ascontiguousarray(np.stack([a[f"L0_attn_{m}_b"][perm].reshape(KC, P) for m in "qk"]).transpose(2, 0, 1))
    gate, up, dn = (a[f"L0_ffn_w_{m}"] for m in ("gate", "up", "down"))
    gu = np.concatenate([gate, up], axis=2).reshape(E, KC, P, 2 * INNER).transpose(0, 2, 1, 3).reshape(E, P, -1)
    dd = dn.reshape(E, INNER // P, P, D).transpose(0, 2, 1, 3).reshape(E, P, -1)
    cos, sin = rope_tables()
    f = np.float32
    arrays = {
        "x": a["L0_attn_x"], "wqk": wqk, "wv": by_rows(a["L0_attn_v_w"].T), "wo": by_rows(a["L0_attn_out_w"].T),
        "bqk": bqk, "bv": a["L0_attn_v_b"], "bo": a["L0_attn_out_b"], "rw": by_rows(a["L0_ffn_router_w"]),
        "rbias": a["L0_ffn_router_bias"], "wexp": np.ascontiguousarray(np.concatenate([gu, dd], axis=2)),
        "swg": by_rows(a["L0_ffn_sw_gate"]), "swu": by_rows(a["L0_ffn_sw_up"]), "swd": by_rows(a["L0_ffn_sw_down"]),
        "cos": cos, "sin": sin, "ident": np.eye(P, dtype=f),
        "before_tok": np.triu(np.ones((P, P), f), 1),
        "before_e": np.tril(np.ones((E, E), f), -1),
        "before_g": np.tril(np.ones((GROUPS, GROUPS), f), -1),
        "iota_p": np.arange(P, dtype=f).reshape(P, 1), "iota_t": np.arange(TILES, dtype=f).reshape(1, TILES),
        "iota_e": np.arange(E, dtype=f) * f(P),
    }
    nc = bacc.Bacc("TRN2", target_bir_lowering=False, num_devices=1)
    ins = {f"in_{k}": np.ascontiguousarray(v) for k, v in arrays.items()}
    aps = [nc.dram_tensor(k, v.shape, mybir.dt.from_np(v.dtype), kind="ExternalInput").ap() for k, v in ins.items()]
    out = nc.dram_tensor("out", (BATCH, SEQ, D), F32, kind="ExternalOutput").ap()
    layer_kernel(nc, *aps, out)
    r = run_bass_kernel_spmd(nc, [ins], core_ids=[0])
    return r.results[0]["out"]
```
